# Optimizing a Trainium2 kernel written in Bass

```python
import numpy as np
import jax
import jax.numpy as jnp

def _softmax(x, axis=-1):
    return jax.nn.softmax(x, axis=axis)

def _gelu(x):
    return jax.nn.gelu(x, approximate=True)

def _silu(x):
    return jax.nn.silu(x)

def _sigmoid(x):
    return jax.nn.sigmoid(x)

def _layernorm(x, axis=-1, eps=1e-05):
    m = jnp.mean(x, axis=axis, keepdims=True)
    v = jnp.var(x, axis=axis, keepdims=True)
    return (x - m) / jnp.sqrt(v + eps)

def _scatter_add(tgt, idx, src, axis=0):
    return tgt.at[idx].add(src)

def _segment_sum(src, seg, n):
    return jax.ops.segment_sum(src, seg, n)
kernel_name = 'mk_adj_resnorm_d1_adj_r2_4f5836'

def setup_inputs(seed: int=0):
    np.random.seed(seed)
    _w = jnp.asarray

    def _rec_inputs():
        import jax
        import jax.numpy as jnp
        _gk = jax.random.key(seed)
        x = -0.0005207 + 1.001 * jax.random.normal(jax.random.fold_in(_gk, 1), (4096, 128), jnp.float32)
        _a = jax.random.bernoulli(jax.random.fold_in(_gk, 2), 0.000976562, (4096, 4096))
        _a = jnp.logical_or(_a, jnp.swapaxes(_a, -1, -2))
        _a = jnp.logical_or(_a, jnp.eye(4096, dtype=bool))
        adj = _a.astype(jnp.int32)
        return (x, adj)
    x, adj = _rec_inputs()

    def _L0_gnn_setup():
        import math
        import jax, jax.numpy as jnp
        import numpy as np
        N = 4096
        F_IN = 128
        F_OUT = 128
        key = jax.random.key(seed)
        ks = jax.random.split(key, 9)
        s = 1.0 / math.sqrt(F_IN)
        return {'x': jax.random.normal(ks[0], (N, F_IN), dtype=jnp.float32), 'adj': jax.random.randint(ks[1], (N, N), 0, 2, dtype=jnp.int32), 'Wq': jax.random.uniform(ks[2], (F_OUT, F_IN), jnp.float32, -s, s), 'bq': jax.random.uniform(ks[3], (F_OUT,), jnp.float32, -s, s), 'Wk': jax.random.uniform(ks[4], (F_OUT, F_IN), jnp.float32, -s, s), 'bk': jax.random.uniform(ks[5], (F_OUT,), jnp.float32, -s, s), 'Wv': jax.random.uniform(ks[6], (F_OUT, F_IN), jnp.float32, -s, s), 'bv': jax.random.uniform(ks[7], (F_OUT,), jnp.float32, -s, s)}
    _L0_gnn_all = _L0_gnn_setup()
    _L0_gnn_in = {k: v for k, v in _L0_gnn_all.items() if k in ('Wq', 'bq', 'Wk', 'bk', 'Wv', 'bv')}
    del _L0_gnn_all
    return {'x': x, 'adj': adj, 'L0_gnn_Wq': _L0_gnn_in['Wq'], 'L0_gnn_bq': _L0_gnn_in['bq'], 'L0_gnn_Wk': _L0_gnn_in['Wk'], 'L0_gnn_bk': _L0_gnn_in['bk'], 'L0_gnn_Wv': _L0_gnn_in['Wv'], 'L0_gnn_bv': _L0_gnn_in['bv']}

def reference(x, adj, L0_gnn_Wq, L0_gnn_bq, L0_gnn_Wk, L0_gnn_bk, L0_gnn_Wv, L0_gnn_bv):
    import jax
    import jax.numpy as jnp

    def _L0_gnn_ref(x, adj, Wq, bq, Wk, bk, Wv, bv):
        import math
        import jax, jax.numpy as jnp
        import numpy as np
        N = 4096
        F_IN = 128
        F_OUT = 128
        q = x @ Wq.T + bq
        k = x @ Wk.T + bk
        v = x @ Wv.T + bv
        d = q.shape[-1]
        scores = q @ k.T / jnp.sqrt(jnp.asarray(d, q.dtype))
        neg = jnp.asarray(-9000000000000000.0, scores.dtype)
        scores = jnp.where(adj > 0, scores, neg)
        attention = jax.nn.softmax(scores, axis=-1)
        att = attention @ v
        return jax.nn.elu(att)
    x = _layernorm(x + _L0_gnn_ref(x, adj, L0_gnn_Wq, L0_gnn_bq, L0_gnn_Wk, L0_gnn_bk, L0_gnn_Wv, L0_gnn_bv), axis=-1)
    return x

_drawn_inputs = setup_inputs


def setup_inputs(seed=0):
    import zlib

    import numpy as np

    out = dict(_drawn_inputs(seed))
    spreads = {}
    factors = {'L0_gnn_bq': 8.0, 'L0_gnn_bk': 8.0}
    for name, (base, spread) in spreads.items():
        noise = np.random.default_rng([zlib.crc32(name.encode()), seed]).standard_normal(out[name].shape)
        drawn = base * np.exp(spread * noise) if base else spread * noise
        out[name] = jnp.asarray(drawn.astype(out[name].dtype))
    for name, factor in factors.items():
        out[name] = (out[name] * factor).astype(out[name].dtype)
    return out
```

```python
from contextlib import ExitStack

import concourse.bass as bass
from concourse import mybir

ALU = mybir.AluOpType
ACT = mybir.ActivationFunctionType
AX_X = mybir.AxisListType.X
F32 = mybir.dt.float32
F16 = mybir.dt.float16
I32 = mybir.dt.int32

P = 128
STEPS = 8
BANK = 512
PIECE = 2 * BANK
MASKED = -9000000000000000.0
EPS = 1e-5
P_SCALE = 2.0 ** 15
LAG_EXP = STEPS + 1
LAG_T = STEPS + 3
LAG_LO = STEPS + 4
LAG_PV = STEPS + 5
PSLOTS = 4
POOL_OPS = 10


def attention_kernel(nc, x, adj, wq, bq, wk, bk, wv, bv, out):
    N, D = x.shape
    TILES = N // P
    PIECES = N // PIECE
    BLOCKS = BANK // P
    SCALE = float(D) ** -0.5
    VW = 2 * D + 2
    assert D == P and N == STEPS * BANK and TILES % 2 == 0

    with ExitStack() as ctx:
        def sb(name, shape, dt):
            return ctx.enter_context(nc.sbuf_tensor(name, shape, dt))

        def psum(name, shape):
            return ctx.enter_context(nc.psum_tensor(name, shape, F32))

        def sem(name):
            return ctx.enter_context(nc.semaphore(name))

        ps_scores = [psum(f"ps_scores{n}", [P, PIECE]) for n in range(2)]
        ps_t = [psum(f"ps_t{n}", [P, BANK]) for n in range(2)]
        ps_out = [psum(f"ps_out{n}", [P, BANK]) for n in range(2)]

        x_rows = sb("x_rows", [P, TILES, D], F32)
        x_t = sb("x_t", [P, N], F32)
        w_rows = sb("w_rows", [P, 3, D], F32)
        w_t = sb("w_t", [P, 3, D], F32)
        b_cols = sb("b_cols", [P, 2], F32)
        bq_scaled = sb("bq_scaled", [P, 1], F32)
        bv_row = sb("bv_row", [1, D], F32)
        ones_row = sb("ones_row", [1, P], F32)
        ident = sb("ident", [P, P], F32)
        q_hi = sb("q_hi", [P, N], F16)
        q_lo = sb("q_lo", [P, N], F16)
        k_hi = sb("k_hi", [P, N], F16)
        k_lo = sb("k_lo", [P, N], F16)
        v_parts = sb("v_parts", [P, TILES, VW], F16)
        adj_sb = [sb(f"adj{n}", [P, N], I32) for n in range(2)]
        mask_sb = [a[:, :].bitcast(F32) for a in adj_sb]
        s_sb = [sb(f"scores{n}", [P, N], F32) for n in range(2)]
        max_parts = sb("max_parts", [P, 2, PIECES], F32)
        neg_max = sb("neg_max", [P, 2], F32)
        p_hi = sb("p_hi", [P, PSLOTS, BANK], F16)
        p_lo = sb("p_lo", [P, PSLOTS, BANK], F16)
        recip = sb("recip", [P, 2], F32)
        att2 = sb("att2", [P, 2, 2 * D], F32)
        att = sb("att", [P, 2, D], F32)
        neg = sb("neg", [P, 2, D], F32)
        pos = sb("pos", [P, 2, D], F32)
        exp_neg = sb("exp_neg", [P, 2, D], F32)
        res = sb("res", [P, 2, D], F32)
        y = sb("y", [P, 2, D], F32)
        act_junk = sb("act_junk", [P, D], F32)
        y_sum = sb("y_sum", [P, 2], F32)
        neg_mean = sb("neg_mean", [P, 2], F32)
        sq_sum = sb("sq_sum", [P, 2], F32)
        var = sb("var", [P, 2], F32)
        rstd = sb("rstd", [P, 2], F32)
        stat_consts = sb("stat_consts", [P, 5], F32)
        expm1 = sb("expm1", [P, 2, D], F32)
        var_eps = sb("var_eps", [P, 2], F32)
        centred = sb("centred", [P, 2, D], F32)
        y_out = sb("y_out", [P, 2, D], F32)

        w_in = sem("w_in")
        x_in = [sem(f"x_in{n}") for n in range(4)]
        consts_set = sem("consts_set")
        ident_set = sem("ident_set")
        wt_ready = sem("wt_ready")
        wt_copied = sem("wt_copied")
        bq_ready = sem("bq_ready")
        xt_ready = sem("xt_ready")
        xt_copied = sem("xt_copied")
        proj_ready = sem("proj_ready")
        proj_hi = sem("proj_hi")
        proj_lo = sem("proj_lo")
        adj_in = [[sem(f"adj_in{n}_{c}") for c in range(PIECES)] for n in range(2)]
        mask_ready = sem("mask_ready")
        scores_ready = sem("scores_ready")
        masked_ready = sem("masked_ready")
        max_ready = sem("max_ready")
        exp_done = sem("exp_done")
        pt_ready = sem("pt_ready")
        phi_ready = sem("phi_ready")
        plo_ready = sem("plo_ready")
        pv_done = sem("pv_done")
        recip_ready = sem("recip_ready")
        att_ready = sem("att_ready")
        relu_ready = sem("relu_ready")
        expneg_ready = sem("expneg_ready")
        ysum_ready = sem("ysum_ready")
        sqsum_ready = sem("sqsum_ready")
        pool_done = sem("pool_done")
        stored = [sem(f"stored{n}") for n in range(2)]

        x_tiled = x.rearrange("(t p) d -> p t d", p=P)
        adj_tiled = adj.rearrange("(t p) m -> t p m", p=P)
        out_tiled = out.rearrange("(t p) d -> t p d", p=P)
        XQ = TILES // 4

        def ps_xt(g):
            return ps_scores[g // 2 % 2][:, g % 2 * BANK:(g % 2 + 1) * BANK]

        def ps_proj(g):
            return (ps_t + ps_out)[g % 4]
        NPROJ = 3 * STEPS

        block = ctx.enter_context(nc.Block())

        @block.sync
        def _(sp):
            sp.dma_start(w_rows[:, 1, :], wk).then_inc(w_in, 16)
            sp.dma_start(w_rows[:, 0, :], wq).then_inc(w_in, 16)
            sp.dma_start(w_rows[:, 2, :], wv).then_inc(w_in, 16)
            for n in range(4):
                sp.dma_start(x_rows[:, n * XQ:(n + 1) * XQ, :], x_tiled[:, n * XQ:(n + 1) * XQ, :]).then_inc(x_in[n], 16)

            def load(i, slot, first):
                for c in range(PIECES):
                    if not first:
                        sp.wait_ge(masked_ready, PIECES * (i - 2) + c + 1)
                    cols = slice(c * PIECE, (c + 1) * PIECE)
                    sp.dma_start(adj_sb[slot][:, cols], adj_tiled[i, :, cols]).then_inc(adj_in[slot][c], 16)

            def store(i, slot):
                sp.wait_ge(pool_done, POOL_OPS * (i + 1))
                sp.dma_start(out_tiled[i], y_out[:, slot, :]).then_inc(stored[slot], 16)

            load(0, 0, True)
            load(1, 1, True)
            load(2, 0, False)
            load(3, 1, False)
            with sp.Fori(1, TILES // 2 - 1) as pair:
                for n in range(2):
                    load(2 * pair + n + 2, n, False)
                    store(2 * pair + n - 2, n)
            for i in range(TILES - 4, TILES):
                store(i, i % 2)
            for n in range(2):
                sp.wait_ge(stored[n], 16 * (TILES // 2))

        @block.gpsimd
        def _(pool):
            nc.gpsimd.memset(ident[:, :], 0.0).then_inc(consts_set, 1)
            nc.gpsimd.memset(ones_row[:, :], 1.0).then_inc(consts_set, 1)
            for n, value in enumerate((-1.0 / D, 1.0 / D, EPS, -0.5, -1.0)):
                nc.gpsimd.memset(stat_consts[:, n:n + 1], value).then_inc(consts_set, 1)
            nc.gpsimd.memset(v_parts[:, :, 2 * D:VW], 1.0).then_inc(consts_set, 1)
            pool.wait_ge(consts_set, 8)
            nc.gpsimd.affine_select(out=ident[:, :], in_=ident[:, :], compare_op=ALU.not_equal, fill=1.0,
                                    base=0, pattern=[[-1, P]], channel_multiplier=1).then_inc(ident_set, 1)

            def finish(i, s):
                done = [POOL_OPS * i]

                def step(ins):
                    done[0] = done[0] + 1
                    ins.then_inc(pool_done, 1)

                def own():
                    pool.wait_ge(pool_done, done[0])

                one = slice(s, s + 1)
                pool.wait_ge(att_ready, i + 1)
                step(nc.gpsimd.tensor_tensor(att[:, s, :], att2[:, s, 0:D], att2[:, s, D:2 * D], ALU.add))
                pool.wait_ge(relu_ready, 2 * i + 1)
                step(nc.gpsimd.tensor_tensor(res[:, s, :], pos[:, s, :], x_rows[:, bass.ds(i, 1), :], ALU.add))
                pool.wait_ge(expneg_ready, i + 1)
                step(nc.gpsimd.tensor_tensor(expm1[:, s, :], exp_neg[:, s, :], stat_consts[:, 4:5].to_broadcast([P, D]), ALU.add))
                own()
                step(nc.gpsimd.tensor_tensor(y[:, s, :], res[:, s, :], expm1[:, s, :], ALU.add))
                pool.wait_ge(ysum_ready, i + 1)
                step(nc.gpsimd.tensor_tensor(neg_mean[:, one], y_sum[:, one], stat_consts[:, 0:1], ALU.mult))
                own()
                step(nc.gpsimd.tensor_tensor(centred[:, s, :], y[:, s, :], neg_mean[:, one].to_broadcast([P, D]), ALU.add))
                pool.wait_ge(sqsum_ready, i + 1)
                step(nc.gpsimd.tensor_tensor(var[:, one], sq_sum[:, one], stat_consts[:, 1:2], ALU.mult))
                own()
                step(nc.gpsimd.tensor_tensor(var_eps[:, one], var[:, one], stat_consts[:, 2:3], ALU.add))
                own()
                step(nc.gpsimd.tensor_tensor(rstd[:, one], var_eps[:, one], stat_consts[:, 3:4], ALU.pow))
                own()
                step(nc.gpsimd.tensor_tensor(y_out[:, s, :], centred[:, s, :], rstd[:, one].to_broadcast([P, D]), ALU.mult))

            def finish_tile(i, s, first):
                if not first:
                    pool.wait_ge(stored[s], 8 * (i - s))
                finish(i, s)

            finish_tile(0, 0, True)
            finish_tile(1, 1, True)
            with pool.Fori(1, TILES // 2) as pair:
                for n in range(2):
                    finish_tile(2 * pair + n, n, False)

        @block.scalar
        def _(act):
            act.dma_start(b_cols[:, 0:1], bq.rearrange("(p a) -> p a", a=1)).then_inc(w_in, 16)
            act.dma_start(b_cols[:, 1:2], bk.rearrange("(p a) -> p a", a=1)).then_inc(w_in, 16)
            act.dma_start(bv_row[:, :], bv.rearrange("(a d) -> a d", a=1)).then_inc(w_in, 16)

            act.wait_ge(wt_ready, 1)
            for n, scale in enumerate((SCALE, 1.0, 1.0)):
                nc.scalar.activation(w_t[:, n, :], ps_t[0][:, n * D:(n + 1) * D], ACT.Copy, scale=scale).then_inc(wt_copied, 1)
            act.wait_ge(w_in, 16 * 6)
            nc.scalar.activation(bq_scaled[:, :], b_cols[:, 0:1], ACT.Copy, scale=SCALE).then_inc(bq_ready, 1)
            for g in range(STEPS):
                act.wait_ge(xt_ready, g + 1)
                nc.scalar.activation(x_t[:, g * BANK:(g + 1) * BANK], ps_xt(g), ACT.Copy).then_inc(xt_copied, 1)
            act.wait_ge(bq_ready, 1)
            for n in range(NPROJ):
                which, g = divmod(n, STEPS)
                cols = slice(g * BANK, (g + 1) * BANK)
                act.wait_ge(proj_ready, n + 1)
                if which == 0:
                    ins = nc.scalar.activation(k_hi[:, cols], ps_proj(n)[:, :], ACT.Identity, bias=b_cols[:, 1:2])
                elif which == 1:
                    ins = nc.scalar.activation(q_hi[:, cols], ps_proj(n)[:, :], ACT.Identity, bias=bq_scaled[:, :])
                else:
                    ins = nc.scalar.activation(v_parts[:, g * BLOCKS:(g + 1) * BLOCKS, D:2 * D],
                                               ps_proj(n)[:, :].rearrange("p (b d) -> p b d", d=D), ACT.Copy)
                ins.then_inc(proj_hi, 1)

            def exp_piece(i, s, c):
                if c == 0:
                    act.wait_ge(max_ready, i + 1)
                cols = slice(c * PIECE, (c + 1) * PIECE)
                nc.scalar.activation(s_sb[s][:, cols], s_sb[s][:, cols], ACT.Exp,
                                     bias=neg_max[:, s:s + 1]).then_inc(exp_done, 1)

            def high_part(i, g, first):
                act.wait_ge(pt_ready, STEPS * i + g + 1)
                if not first:
                    act.wait_ge(pv_done, STEPS * i + g + 1 - PSLOTS)
                nc.scalar.activation(p_hi[:, g % PSLOTS, :], ps_t[g % 2][:, :], ACT.Copy, scale=P_SCALE).then_inc(phi_ready, 1)

            def attention(i, s):
                act.wait_ge(recip_ready, i + 1)
                nc.scalar.activation(att2[:, s, :], ps_out[s][:, 0:2 * D], ACT.Copy, scale=recip[:, s:s + 1]).then_inc(att_ready, 1)

            def elu_exp(i, s):
                act.wait_ge(pool_done, POOL_OPS * i + 1)
                nc.scalar.activation(pos[:, s, :], att[:, s, :], ACT.Relu).then_inc(relu_ready, 1)
                nc.scalar.activation(neg[:, s, :], att[:, s, :], ACT.Relu, scale=-1.0).then_inc(relu_ready, 1)
                act.wait_ge(relu_ready, 2 * i + 2)
                nc.scalar.activation(exp_neg[:, s, :], neg[:, s, :], ACT.Exp, scale=-1.0).then_inc(expneg_ready, 1)

            def row_sum(i, s):
                act.wait_ge(pool_done, POOL_OPS * i + 4)
                nc.scalar.activation(act_junk[:, :], y[:, s, :], ACT.Copy, accum_out=y_sum[:, s:s + 1]).then_inc(ysum_ready, 1)

            def square_sum(i, s):
                act.wait_ge(pool_done, POOL_OPS * i + 5)
                nc.scalar.activation(act_junk[:, :], y[:, s, :], ACT.Square, bias=neg_mean[:, s:s + 1],
                                     accum_out=sq_sum[:, s:s + 1]).then_inc(sqsum_ready, 1)

            def period(i, s, has_exp=True, has_last=True, has_first=True, warm=True):
                for j in range(STEPS):
                    g = (j - LAG_T) % STEPS
                    if j < LAG_T - STEPS and has_last:
                        high_part(i - 2, g, False)
                    if j >= LAG_T - STEPS and has_first:
                        high_part(i - 1, g, not warm and g < PSLOTS)
                    if has_last:
                        if j == 5:
                            attention(i - 2, s)
                        if j == 6:
                            elu_exp(i - 2, s)
                        if j == 7:
                            row_sum(i - 2, s)
                    if j % 2 == 1 and has_exp:
                        exp_piece(i - 1, 1 - s, j // 2)
                    if has_last and j == 7:
                        square_sum(i - 2, s)

            period(1, 1, has_last=False, warm=False)
            with act.Fori(1, TILES // 2) as pair:
                for n in range(2):
                    period(2 * pair + n, n)
            period(TILES, 0, has_exp=True)
            period(TILES + 1, 1, has_exp=False, has_first=False)

        @block.vector
        def _(dve):
            for n in range(NPROJ):
                which, g = divmod(n, STEPS)
                cols = slice(g * BANK, (g + 1) * BANK)
                dve.wait_ge(proj_hi, n + 1)
                if which == 0:
                    ins = nc.vector.scalar_tensor_tensor(out=k_lo[:, cols], in0=ps_proj(n)[:, :], scalar=b_cols[:, 1:2],
                                                         in1=k_hi[:, cols], op0=ALU.add, op1=ALU.subtract)
                elif which == 1:
                    ins = nc.vector.scalar_tensor_tensor(out=q_lo[:, cols], in0=ps_proj(n)[:, :], scalar=bq_scaled[:, :],
                                                         in1=q_hi[:, cols], op0=ALU.add, op1=ALU.subtract)
                else:
                    rows = slice(g * BLOCKS, (g + 1) * BLOCKS)
                    ins = nc.vector.tensor_tensor(v_parts[:, rows, 0:D], ps_proj(n)[:, :].rearrange("p (b d) -> p b d", d=D),
                                                  v_parts[:, rows, D:2 * D], ALU.subtract)
                ins.then_inc(proj_lo, 1)

            def mask_piece(i, s, c):
                cols = slice(c * PIECE, (c + 1) * PIECE)
                dve.wait_ge(adj_in[s][c], 8 * (i - s) + 16)
                nc.vector.tensor_scalar(mask_sb[s][:, cols], adj_sb[s][:, cols], 0.0, MASKED,
                                        ALU.is_le, ALU.mult).then_inc(mask_ready, 1)

            def masked_piece(i, s, c, first, last_tile):
                cols = slice(c * PIECE, (c + 1) * PIECE)
                if not first:
                    dve.wait_ge(pt_ready, STEPS * (i - 2) + 2 * c + 2)
                dve.wait_ge(mask_ready, PIECES * i + c + 1)
                dve.wait_ge(scores_ready, PIECES * i + c + 1)
                if c < PIECES - 1:
                    mask_piece(i, s, c + 1)
                elif not last_tile:
                    mask_piece(i + 1, 1 - s, 0)
                nc.vector.tensor_tensor_reduce(out=s_sb[s][:, cols], in0=ps_scores[c % 2][:, :], in1=mask_sb[s][:, cols],
                                               scale=1.0, scalar=-3.0e38, op0=ALU.add, op1=ALU.max,
                                               accum_out=max_parts[:, s, c:c + 1]).then_inc(masked_ready, 1)

            def row_max(i, s):
                dve.wait_ge(masked_ready, PIECES * (i + 1))
                nc.vector.tensor_reduce(neg_max[:, s:s + 1], max_parts[:, s, :], AX_X, ALU.max,
                                        negate=True).then_inc(max_ready, 1)

            def low_part(i, g):
                dve.wait_ge(phi_ready, STEPS * i + g + 1)
                nc.vector.scalar_tensor_tensor(out=p_lo[:, g % PSLOTS, :], in0=ps_t[g % 2][:, :], scalar=P_SCALE,
                                               in1=p_hi[:, g % PSLOTS, :], op0=ALU.mult, op1=ALU.subtract).then_inc(plo_ready, 1)

            def reciprocal(i, s):
                dve.wait_ge(pv_done, STEPS * (i + 1))
                nc.vector.reciprocal(recip[:, s:s + 1], ps_out[s][:, 2 * D:2 * D + 1]).then_inc(recip_ready, 1)

            def period(i, s, has_scores=True, has_last=True, has_first=True, warm=True, last_tile=False):
                for j in range(STEPS):
                    g = (j - LAG_LO) % STEPS
                    if j < LAG_LO - STEPS and has_last:
                        low_part(i - 2, g)
                    if j >= LAG_LO - STEPS and has_first:
                        low_part(i - 1, g)
                    if j == 5 and has_last:
                        reciprocal(i - 2, s)
                    if has_scores:
                        if j % 2 == 1:
                            masked_piece(i, s, j // 2, not warm, last_tile)
                        if j == STEPS - 1:
                            row_max(i, s)

            mask_piece(0, 0, 0)
            period(0, 0, has_last=False, has_first=False, warm=False)
            period(1, 1, has_last=False, warm=False)
            with dve.Fori(1, TILES // 2 - 1) as pair:
                for n in range(2):
                    period(2 * pair + n, n)
            period(TILES - 2, 0)
            period(TILES - 1, 1, last_tile=True)
            period(TILES, 0, has_scores=False)
            period(TILES + 1, 1, has_scores=False, has_first=False)

        @block.tensor
        def _(pe):
            pe.wait_ge(ident_set, 1)
            pe.wait_ge(w_in, 16 * 6)
            for n in range(3):
                last = nc.tensor.transpose(ps_t[0][:, n * D:(n + 1) * D], w_rows[:, n, :], ident[:, :])
            last.then_inc(wt_ready, 1)
            for g in range(STEPS):
                if g % 2 == 0:
                    pe.wait_ge(x_in[g // 2], 16)
                if g >= 4:
                    pe.wait_ge(xt_copied, g - 3)
                for b in range(BLOCKS):
                    last = nc.tensor.transpose(ps_xt(g)[:, b * P:(b + 1) * P], x_rows[:, g * BLOCKS + b, :], ident[:, :])
                last.then_inc(xt_ready, 1)
            pe.wait_ge(wt_copied, 3)
            for n in range(NPROJ):
                which, g = divmod(n, STEPS)
                if which == 0:
                    pe.wait_ge(xt_copied, g + 1)
                if n >= 4:
                    pe.wait_ge(proj_lo, n - 3)
                if which < 2:
                    last = nc.tensor.matmul(ps_proj(n)[:, :], w_t[:, 1 - which, :], x_t[:, g * BANK:(g + 1) * BANK],
                                            start=True, stop=True)
                else:
                    for b in range(BLOCKS):
                        t = g * BLOCKS + b
                        nc.tensor.matmul(ps_proj(n)[:, b * D:(b + 1) * D], x_t[:, t * P:(t + 1) * P], w_t[:, 2, :],
                                         start=True, stop=False)
                        last = nc.tensor.matmul(ps_proj(n)[:, b * D:(b + 1) * D], ones_row[:, :], bv_row[:, :],
                                                start=False, stop=True)
                last.then_inc(proj_ready, 1)

            def scores(i, j, first):
                c = j // 2
                place = ps_scores[c % 2][:, j % 2 * BANK:(j % 2 + 1) * BANK]
                cols = slice(j * BANK, (j + 1) * BANK)
                rows = bass.ds(i * P, P)
                if j % 2 == 0 and not (first and c < 2):
                    pe.wait_ge(masked_ready, PIECES * i + c - 1)
                nc.tensor.matmul(place, q_hi[:, rows], k_hi[:, cols], start=True, stop=False)
                nc.tensor.matmul(place, q_hi[:, rows], k_lo[:, cols], start=False, stop=False)
                last = nc.tensor.matmul(place, q_lo[:, rows], k_hi[:, cols], start=False, stop=True)
                if j % 2 == 1:
                    last.then_inc(scores_ready, 1)

            def transposes(i, s, g, first):
                pe.wait_ge(exp_done, PIECES * i + g // 2 + 1)
                if not (first and g < 2):
                    pe.wait_ge(plo_ready, STEPS * i + g - 1)
                for b in range(BLOCKS):
                    k = g * BLOCKS + b
                    last = nc.tensor.transpose(ps_t[g % 2][:, b * P:(b + 1) * P], s_sb[s][:, k * P:(k + 1) * P], ident[:, :])
                last.then_inc(pt_ready, 1)

            def values(i, s, g):
                pe.wait_ge(plo_ready, STEPS * i + g + 1)
                for b in range(BLOCKS):
                    k = g * BLOCKS + b
                    blk = slice(b * P, (b + 1) * P)
                    nc.tensor.matmul(ps_out[s][:, 0:2 * D + 1], p_hi[:, g % PSLOTS, blk], v_parts[:, k, 0:2 * D + 1],
                                     start=(k == 0), stop=False)
                    last = nc.tensor.matmul(ps_out[s][:, D:2 * D + 1], p_lo[:, g % PSLOTS, blk], v_parts[:, k, D:2 * D + 1],
                                            start=False, stop=(k == TILES - 1))
                last.then_inc(pv_done, 1)

            def period(i, s, has_scores=True, has_last=True, has_first=True, warm=True):
                for j in range(STEPS):
                    if has_scores:
                        scores(i, j, not warm and s == 0)
                    g = (j - LAG_T) % STEPS
                    if j < LAG_T - STEPS and has_last:
                        transposes(i - 2, s, g, False)
                    if j >= LAG_T - STEPS and has_first:
                        transposes(i - 1, 1 - s, g, not warm)
                    g = (j - LAG_PV) % STEPS
                    if j < LAG_PV - STEPS and has_last:
                        values(i - 2, s, g)
                    if j >= LAG_PV - STEPS and has_first:
                        values(i - 1, 1 - s, g)

            pe.wait_ge(proj_lo, NPROJ)
            period(0, 0, has_last=False, has_first=False, warm=False)
            period(1, 1, has_last=False, warm=False)
            with pe.Fori(1, TILES // 2) as pair:
                for n in range(2):
                    period(2 * pair + n, n)
            period(TILES, 0, has_scores=False)
            period(TILES + 1, 1, has_scores=False, has_first=False)


_INS = ["x", "adj", "L0_gnn_Wq", "L0_gnn_bq", "L0_gnn_Wk", "L0_gnn_bk", "L0_gnn_Wv", "L0_gnn_bv"]


def kernel(**inputs):
    import numpy as _np
    import concourse.bacc as _bacc
    from concourse.bass_utils import run_bass_kernel_spmd as _run

    nc = _bacc.Bacc("TRN2", target_bir_lowering=False, num_devices=1)
    arrays, args = {}, []
    for name in _INS:
        a = _np.ascontiguousarray(inputs[name])
        arrays[f"in_{name}_dram"] = a
        args.append(nc.dram_tensor(f"in_{name}_dram", a.shape, mybir.dt.from_np(a.dtype), kind="ExternalInput").ap())
    out = nc.dram_tensor("out_0_dram", inputs["x"].shape, F32, kind="ExternalOutput").ap()
    attention_kernel(nc, *args, out)
    r = _run(nc, [arrays], core_ids=[0])
    return r.results[0]["out_0_dram"]
```

```python
from contextlib import ExitStack

import concourse.bass as bass
from concourse import mybir

ALU = mybir.AluOpType
ACT = mybir.ActivationFunctionType
AX_X = mybir.AxisListType.X
F32 = mybir.dt.float32
F16 = mybir.dt.float16
I32 = mybir.dt.int32

P = 128
STEPS = 8
BANK = 512
PIECE = 2 * BANK
MASKED = -9000000000000000.0
EPS = 1e-5
P_SCALE = 2.0 ** 15
LAG_T = STEPS + 3
LAG_LO = STEPS + 4
LAG_PV = STEPS + 5
PSLOTS = 4
POOL_OPS = 11


def attention_kernel(nc, x, adj, wq, bq, wk, bk, wv, bv, out):
    N, D = x.shape
    TILES = N // P
    PIECES = N // PIECE
    BLOCKS = BANK // P
    SCALE = float(D) ** -0.5
    VW = 2 * D + 2
    assert D == P and N == STEPS * BANK and TILES % 2 == 0

    with ExitStack() as ctx:
        def sb(name, shape, dt):
            return ctx.enter_context(nc.sbuf_tensor(name, shape, dt))

        def psum(name, shape):
            return ctx.enter_context(nc.psum_tensor(name, shape, F32))

        def sem(name):
            return ctx.enter_context(nc.semaphore(name))

        ps_scores = [psum(f"ps_scores{n}", [P, PIECE]) for n in range(2)]
        ps_t = [psum(f"ps_t{n}", [P, BANK]) for n in range(2)]
        ps_out = [psum(f"ps_out{n}", [P, BANK]) for n in range(2)]

        x_rows = sb("x_rows", [P, TILES, D], F32)
        x_t = sb("x_t", [P, N], F32)
        w_rows = sb("w_rows", [P, 3, D], F32)
        w_t = sb("w_t", [P, 3, D], F32)
        b_cols = sb("b_cols", [P, 2], F32)
        bq_scaled = sb("bq_scaled", [P, 1], F32)
        bv_rows = sb("bv_rows", [P, D], F32)
        ident = sb("ident", [P, P], F32)
        q_hi = sb("q_hi", [P, N], F16)
        q_lo = sb("q_lo", [P, N], F16)
        k_hi = sb("k_hi", [P, N], F16)
        k_lo = sb("k_lo", [P, N], F16)
        v_parts = sb("v_parts", [P, TILES, VW], F16)
        adj_sb = [sb(f"adj{n}", [P, N], I32) for n in range(2)]
        mask_sb = [a[:, :].bitcast(F32) for a in adj_sb]
        s_sb = [sb(f"scores{n}", [P, N], F32) for n in range(2)]
        max_parts = sb("max_parts", [P, 2, PIECES], F32)
        neg_max = sb("neg_max", [P, 2], F32)
        p_hi = sb("p_hi", [P, PSLOTS, BANK], F16)
        p_lo = sb("p_lo", [P, PSLOTS, BANK], F16)
        recip = sb("recip", [P, 2], F32)
        att2 = sb("att2", [P, 2, 2 * D], F32)
        att_sum = sb("att_sum", [P, 2, D], F32)
        att = sb("att", [P, 2, D], F32)
        neg = sb("neg", [P, 2, D], F32)
        pos = sb("pos", [P, 2, D], F32)
        exp_neg = sb("exp_neg", [P, 2, D], F32)
        res = sb("res", [P, 2, D], F32)
        y = sb("y", [P, 2, D], F32)
        act_junk = sb("act_junk", [P, D], F32)
        y_sum = sb("y_sum", [P, 2], F32)
        neg_mean = sb("neg_mean", [P, 2], F32)
        sq_sum = sb("sq_sum", [P, 2], F32)
        var = sb("var", [P, 2], F32)
        rstd = sb("rstd", [P, 2], F32)
        stat_consts = sb("stat_consts", [P, 5], F32)
        expm1 = sb("expm1", [P, 2, D], F32)
        var_eps = sb("var_eps", [P, 2], F32)
        centred = sb("centred", [P, 2, D], F32)
        y_out = sb("y_out", [P, 2, D], F32)

        w_in = sem("w_in")
        b_in = sem("b_in")
        bv_in = sem("bv_in")
        x_in = [sem(f"x_in{n}") for n in range(4)]
        consts_set = sem("consts_set")
        ident_set = sem("ident_set")
        wt_ready = sem("wt_ready")
        wt_copied = sem("wt_copied")
        bq_ready = sem("bq_ready")
        xt_ready = sem("xt_ready")
        xt_copied = sem("xt_copied")
        proj_ready = sem("proj_ready")
        proj_hi = sem("proj_hi")
        proj_lo = sem("proj_lo")
        adj_in = [[sem(f"adj_in{n}_{c}") for c in range(PIECES)] for n in range(2)]
        mask_ready = sem("mask_ready")
        scores_ready = sem("scores_ready")
        masked_ready = sem("masked_ready")
        max_ready = sem("max_ready")
        exp_done = sem("exp_done")
        pt_ready = sem("pt_ready")
        phi_ready = sem("phi_ready")
        plo_ready = sem("plo_ready")
        pv_done = sem("pv_done")
        recip_ready = sem("recip_ready")
        att_ready = sem("att_ready")
        relu_ready = sem("relu_ready")
        expneg_ready = sem("expneg_ready")
        ysum_ready = sem("ysum_ready")
        sqsum_ready = sem("sqsum_ready")
        pool_done = sem("pool_done")
        stored = [sem(f"stored{n}") for n in range(2)]

        x_tiled = x.rearrange("(t p) d -> p t d", p=P)
        adj_tiled = adj.rearrange("(t p) m -> t p m", p=P)
        out_tiled = out.rearrange("(t p) d -> t p d", p=P)
        XQ = TILES // 4

        def ps_xt(g):
            return ps_scores[g // 2 % 2][:, g % 2 * BANK:(g % 2 + 1) * BANK]

        ps_proj = ps_t + ps_out
        proj = [("q", 0, 3)] + [("k", g, g % 4) for g in range(STEPS)]
        proj_of_step = {}
        for t in range(STEPS + 3):
            proj_of_step[t] = []
            if t < STEPS:
                proj_of_step[t].append(len(proj))
                proj.append(("v", t, 2 + t % 2))
            if t >= 4:
                proj_of_step[t].append(len(proj))
                proj.append(("q", t - 3, (t - 3) % 2))
        AHEAD = STEPS + 1

        def user_before(n):
            return max([m + 1 for m in range(n) if proj[m][2] == proj[n][2]], default=0)

        block = ctx.enter_context(nc.Block())

        @block.sync
        def _(sp):
            for n in range(4):
                if n == 1:
                    sp.dma_start(w_rows[:, 1, :], wk).then_inc(w_in, 16)
                    sp.dma_start(w_rows[:, 0, :], wq).then_inc(w_in, 16)
                    sp.dma_start(w_rows[:, 2, :], wv).then_inc(w_in, 16)
                sp.dma_start(x_rows[:, n * XQ:(n + 1) * XQ, :], x_tiled[:, n * XQ:(n + 1) * XQ, :]).then_inc(x_in[n], 16)

            def load(i, slot, first):
                for c in range(PIECES):
                    if not first:
                        sp.wait_ge(masked_ready, PIECES * (i - 2) + c + 1)
                    cols = slice(c * PIECE, (c + 1) * PIECE)
                    sp.dma_start(adj_sb[slot][:, cols], adj_tiled[i, :, cols]).then_inc(adj_in[slot][c], 16)

            def store(i, slot):
                sp.wait_ge(pool_done, POOL_OPS * (i + 1))
                sp.dma_start(out_tiled[i], y_out[:, slot, :]).then_inc(stored[slot], 16)

            load(0, 0, True)
            load(1, 1, True)
            load(2, 0, False)
            load(3, 1, False)
            with sp.Fori(1, TILES // 2 - 1) as pair:
                for n in range(2):
                    load(2 * pair + n + 2, n, False)
                    store(2 * pair + n - 2, n)
            for i in range(TILES - 4, TILES):
                store(i, i % 2)
            for n in range(2):
                sp.wait_ge(stored[n], 16 * (TILES // 2))

        @block.gpsimd
        def _(pool):
            nc.gpsimd.memset(ident[:, :], 0.0).then_inc(consts_set, 1)
            for n, value in enumerate((-1.0 / D, 1.0 / D, EPS, -0.5, -1.0)):
                nc.gpsimd.memset(stat_consts[:, n:n + 1], value).then_inc(consts_set, 1)
            nc.gpsimd.memset(v_parts[:, :, 2 * D:VW], 1.0).then_inc(consts_set, 1)
            pool.wait_ge(consts_set, 7)
            nc.gpsimd.affine_select(out=ident[:, :], in_=ident[:, :], compare_op=ALU.not_equal, fill=1.0,
                                    base=0, pattern=[[-1, P]], channel_multiplier=1).then_inc(ident_set, 1)

            def finish(i, s):
                done = [POOL_OPS * i]

                def step(ins):
                    done[0] = done[0] + 1
                    ins.then_inc(pool_done, 1)

                def own():
                    pool.wait_ge(pool_done, done[0])

                one = slice(s, s + 1)
                pool.wait_ge(att_ready, i + 1)
                step(nc.gpsimd.tensor_tensor(att_sum[:, s, :], att2[:, s, 0:D], att2[:, s, D:2 * D], ALU.add))
                own()
                step(nc.gpsimd.tensor_tensor(att[:, s, :], att_sum[:, s, :], bv_rows[:, :], ALU.add))
                pool.wait_ge(relu_ready, 2 * i + 1)
                step(nc.gpsimd.tensor_tensor(res[:, s, :], pos[:, s, :], x_rows[:, bass.ds(i, 1), :], ALU.add))
                pool.wait_ge(expneg_ready, i + 1)
                step(nc.gpsimd.tensor_tensor(expm1[:, s, :], exp_neg[:, s, :], stat_consts[:, 4:5].to_broadcast([P, D]), ALU.add))
                own()
                step(nc.gpsimd.tensor_tensor(y[:, s, :], res[:, s, :], expm1[:, s, :], ALU.add))
                pool.wait_ge(ysum_ready, i + 1)
                step(nc.gpsimd.tensor_tensor(neg_mean[:, one], y_sum[:, one], stat_consts[:, 0:1], ALU.mult))
                own()
                step(nc.gpsimd.tensor_tensor(centred[:, s, :], y[:, s, :], neg_mean[:, one].to_broadcast([P, D]), ALU.add))
                pool.wait_ge(sqsum_ready, i + 1)
                step(nc.gpsimd.tensor_tensor(var[:, one], sq_sum[:, one], stat_consts[:, 1:2], ALU.mult))
                own()
                step(nc.gpsimd.tensor_tensor(var_eps[:, one], var[:, one], stat_consts[:, 2:3], ALU.add))
                own()
                step(nc.gpsimd.tensor_tensor(rstd[:, one], var_eps[:, one], stat_consts[:, 3:4], ALU.pow))
                own()
                step(nc.gpsimd.tensor_tensor(y_out[:, s, :], centred[:, s, :], rstd[:, one].to_broadcast([P, D]), ALU.mult))

            def finish_tile(i, s, first):
                if not first:
                    pool.wait_ge(stored[s], 8 * (i - s))
                finish(i, s)

            pool.wait_ge(bv_in, 16)
            finish_tile(0, 0, True)
            finish_tile(1, 1, True)
            with pool.Fori(1, TILES // 2) as pair:
                for n in range(2):
                    finish_tile(2 * pair + n, n, False)

        @block.scalar
        def _(act):
            act.dma_start(b_cols[:, 0:1], bq.rearrange("(p a) -> p a", a=1)).then_inc(b_in, 16)
            act.dma_start(b_cols[:, 1:2], bk.rearrange("(p a) -> p a", a=1)).then_inc(b_in, 16)
            act.dma_start(bv_rows[:, :], bv.rearrange("(a d) -> a d", a=1).to_broadcast([P, D])).then_inc(bv_in, 16)

            act.wait_ge(wt_ready, 1)
            for n, scale in enumerate((SCALE, 1.0, 1.0)):
                nc.scalar.activation(w_t[:, n, :], ps_t[0][:, n * D:(n + 1) * D], ACT.Copy, scale=scale).then_inc(wt_copied, 1)
            act.wait_ge(b_in, 16 * 2)
            nc.scalar.activation(bq_scaled[:, :], b_cols[:, 0:1], ACT.Copy, scale=SCALE).then_inc(bq_ready, 1)

            def high_of_projection(n):
                which, g, bank = proj[n]
                cols = slice(g * BANK, (g + 1) * BANK)
                act.wait_ge(proj_ready, n + 1)
                if which == "k":
                    ins = nc.scalar.activation(k_hi[:, cols], ps_proj[bank][:, :], ACT.Identity, bias=b_cols[:, 1:2])
                elif which == "q":
                    ins = nc.scalar.activation(q_hi[:, cols], ps_proj[bank][:, :], ACT.Identity, bias=bq_scaled[:, :])
                else:
                    ins = nc.scalar.activation(v_parts[:, g * BLOCKS:(g + 1) * BLOCKS, D:2 * D],
                                               ps_proj[bank][:, :].rearrange("p (b d) -> p b d", d=D), ACT.Copy)
                ins.then_inc(proj_hi, 1)

            act.wait_ge(bq_ready, 1)
            for g in range(STEPS):
                act.wait_ge(xt_ready, g + 1)
                nc.scalar.activation(x_t[:, g * BANK:(g + 1) * BANK], ps_xt(g), ACT.Copy).then_inc(xt_copied, 1)
                if g == 1:
                    high_of_projection(0)
                if g > 0:
                    high_of_projection(g)
            high_of_projection(STEPS)

            def exp_piece(i, s, c):
                if c == 0:
                    act.wait_ge(max_ready, i + 1)
                cols = slice(c * PIECE, (c + 1) * PIECE)
                nc.scalar.activation(s_sb[s][:, cols], s_sb[s][:, cols], ACT.Exp,
                                     bias=neg_max[:, s:s + 1]).then_inc(exp_done, 1)

            def high_part(i, g, first):
                act.wait_ge(pt_ready, STEPS * i + g + 1)
                if not first:
                    act.wait_ge(pv_done, STEPS * i + g + 1 - PSLOTS)
                nc.scalar.activation(p_hi[:, g % PSLOTS, :], ps_t[g % 2][:, :], ACT.Copy, scale=P_SCALE).then_inc(phi_ready, 1)

            def attention(i, s):
                act.wait_ge(recip_ready, i + 1)
                nc.scalar.activation(att2[:, s, :], ps_out[s][:, 0:2 * D], ACT.Copy, scale=recip[:, s:s + 1]).then_inc(att_ready, 1)

            def elu_exp(i, s):
                act.wait_ge(pool_done, POOL_OPS * i + 2)
                nc.scalar.activation(pos[:, s, :], att[:, s, :], ACT.Relu).then_inc(relu_ready, 1)
                nc.scalar.activation(neg[:, s, :], att[:, s, :], ACT.Relu, scale=-1.0).then_inc(relu_ready, 1)
                act.wait_ge(relu_ready, 2 * i + 2)
                nc.scalar.activation(exp_neg[:, s, :], neg[:, s, :], ACT.Exp, scale=-1.0).then_inc(expneg_ready, 1)

            def row_sum(i, s):
                act.wait_ge(pool_done, POOL_OPS * i + 5)
                nc.scalar.activation(act_junk[:, :], y[:, s, :], ACT.Copy, accum_out=y_sum[:, s:s + 1]).then_inc(ysum_ready, 1)

            def square_sum(i, s):
                act.wait_ge(pool_done, POOL_OPS * i + 6)
                nc.scalar.activation(act_junk[:, :], y[:, s, :], ACT.Square, bias=neg_mean[:, s:s + 1],
                                     accum_out=sq_sum[:, s:s + 1]).then_inc(sqsum_ready, 1)

            def period(i, s, has_exp=True, has_last=True, has_first=True, warm=True, ends=((0, 5),)):
                for j in range(STEPS):
                    if not warm:
                        for n in proj_of_step.get(STEPS * i + j, ()):
                            high_of_projection(n)
                    g = (j - LAG_T) % STEPS
                    if j < LAG_T - STEPS and has_last:
                        high_part(i - 2, g, False)
                    if j >= LAG_T - STEPS and has_first:
                        high_part(i - 1, g, not warm and g < PSLOTS)
                    for back, step in ends:
                        if has_last:
                            ending = (i - 2 - back, s ^ (back % 2))
                            if j == step:
                                attention(*ending)
                            if j == step + 1:
                                elu_exp(*ending)
                            if j == step + 2:
                                row_sum(*ending)
                    if j % 2 == 1 and has_exp:
                        exp_piece(i - 1, 1 - s, j // 2)
                    for back, step in ends:
                        if has_last and j == step + 2:
                            square_sum(i - 2 - back, s ^ (back % 2))

            period(0, 0, has_exp=False, has_last=False, has_first=False, warm=False)
            period(1, 1, has_last=False, warm=False)
            with act.Fori(1, TILES // 2) as pair:
                for n in range(2):
                    period(2 * pair + n, n)
            period(TILES, 0, ends=())
            period(TILES + 1, 1, has_exp=False, has_first=False, ends=((1, 0), (0, 5)))

        @block.vector
        def _(dve):
            def low_of_projection(n):
                which, g, bank = proj[n]
                cols = slice(g * BANK, (g + 1) * BANK)
                dve.wait_ge(proj_hi, n + 1)
                if which == "k":
                    ins = nc.vector.scalar_tensor_tensor(out=k_lo[:, cols], in0=ps_proj[bank][:, :], scalar=b_cols[:, 1:2],
                                                         in1=k_hi[:, cols], op0=ALU.add, op1=ALU.subtract)
                elif which == "q":
                    ins = nc.vector.scalar_tensor_tensor(out=q_lo[:, cols], in0=ps_proj[bank][:, :], scalar=bq_scaled[:, :],
                                                         in1=q_hi[:, cols], op0=ALU.add, op1=ALU.subtract)
                else:
                    rows = slice(g * BLOCKS, (g + 1) * BLOCKS)
                    ins = nc.vector.tensor_tensor(v_parts[:, rows, 0:D], ps_proj[bank][:, :].rearrange("p (b d) -> p b d", d=D),
                                                  v_parts[:, rows, D:2 * D], ALU.subtract)
                ins.then_inc(proj_lo, 1)

            def mask_piece(i, s, c):
                cols = slice(c * PIECE, (c + 1) * PIECE)
                dve.wait_ge(adj_in[s][c], 8 * (i - s) + 16)
                nc.vector.tensor_scalar(mask_sb[s][:, cols], adj_sb[s][:, cols], 0.0, MASKED,
                                        ALU.is_le, ALU.mult).then_inc(mask_ready, 1)

            def masked_piece(i, s, c, first, last_tile):
                cols = slice(c * PIECE, (c + 1) * PIECE)
                if not first:
                    dve.wait_ge(pt_ready, STEPS * (i - 2) + 2 * c + 2)
                dve.wait_ge(mask_ready, PIECES * i + c + 1)
                dve.wait_ge(scores_ready, PIECES * i + c + 1)
                if not last_tile:
                    mask_piece(i + 1, 1 - s, c)
                nc.vector.tensor_tensor_reduce(out=s_sb[s][:, cols], in0=ps_scores[c % 2][:, :], in1=mask_sb[s][:, cols],
                                               scale=1.0, scalar=-3.0e38, op0=ALU.add, op1=ALU.max,
                                               accum_out=max_parts[:, s, c:c + 1]).then_inc(masked_ready, 1)

            def row_max(i, s):
                dve.wait_ge(masked_ready, PIECES * (i + 1))
                nc.vector.tensor_reduce(neg_max[:, s:s + 1], max_parts[:, s, :], AX_X, ALU.max,
                                        negate=True).then_inc(max_ready, 1)

            def low_part(i, g):
                dve.wait_ge(phi_ready, STEPS * i + g + 1)
                nc.vector.scalar_tensor_tensor(out=p_lo[:, g % PSLOTS, :], in0=ps_t[g % 2][:, :], scalar=P_SCALE,
                                               in1=p_hi[:, g % PSLOTS, :], op0=ALU.mult, op1=ALU.subtract).then_inc(plo_ready, 1)

            def reciprocal(i, s):
                dve.wait_ge(pv_done, STEPS * (i + 1))
                nc.vector.reciprocal(recip[:, s:s + 1], ps_out[s][:, 2 * D:2 * D + 1]).then_inc(recip_ready, 1)

            def period(i, s, has_scores=True, has_last=True, has_first=True, warm=True, last_tile=False):
                for j in range(STEPS):
                    if not warm:
                        for n in proj_of_step.get(STEPS * i + j, ()):
                            low_of_projection(n)
                    g = (j - LAG_LO) % STEPS
                    if j < LAG_LO - STEPS and has_last:
                        low_part(i - 2, g)
                    if j >= LAG_LO - STEPS and has_first:
                        low_part(i - 1, g)
                    if j == 5 and has_last:
                        reciprocal(i - 2, s)
                    if has_scores:
                        if j % 2 == 1:
                            masked_piece(i, s, j // 2, not warm, last_tile)
                        if j == STEPS - 1:
                            row_max(i, s)

            for n in range(AHEAD):
                low_of_projection(n)
                if n >= AHEAD - PIECES:
                    mask_piece(0, 0, n - AHEAD + PIECES)
            period(0, 0, has_last=False, has_first=False, warm=False)
            period(1, 1, has_last=False, warm=False)
            with dve.Fori(1, TILES // 2 - 1) as pair:
                for n in range(2):
                    period(2 * pair + n, n)
            period(TILES - 2, 0)
            period(TILES - 1, 1, last_tile=True)
            period(TILES, 0, has_scores=False)
            period(TILES + 1, 1, has_scores=False, has_first=False)

        @block.tensor
        def _(pe):
            def project(n):
                which, g, bank = proj[n]
                if user_before(n):
                    pe.wait_ge(proj_lo, user_before(n))
                if which == "v":
                    for b in range(BLOCKS):
                        t = g * BLOCKS + b
                        last = nc.tensor.matmul(ps_proj[bank][:, b * D:(b + 1) * D], x_t[:, t * P:(t + 1) * P], w_t[:, 2, :],
                                                start=True, stop=True)
                else:
                    last = nc.tensor.matmul(ps_proj[bank][:, :], w_t[:, "qk".index(which), :], x_t[:, g * BANK:(g + 1) * BANK],
                                            start=True, stop=True)
                last.then_inc(proj_ready, 1)

            pe.wait_ge(ident_set, 1)
            for g in range(STEPS):
                if g % 2 == 0:
                    pe.wait_ge(x_in[g // 2], 16)
                if g >= 4:
                    pe.wait_ge(xt_copied, g - 3)
                for b in range(BLOCKS):
                    last = nc.tensor.transpose(ps_xt(g)[:, b * P:(b + 1) * P], x_rows[:, g * BLOCKS + b, :], ident[:, :])
                last.then_inc(xt_ready, 1)
                if g == 0:
                    pe.wait_ge(w_in, 16 * 3)
                    for n in range(3):
                        last = nc.tensor.transpose(ps_t[0][:, n * D:(n + 1) * D], w_rows[:, n, :], ident[:, :])
                    last.then_inc(wt_ready, 1)
                if g > 0:
                    if g == 1:
                        pe.wait_ge(wt_copied, 3)
                    pe.wait_ge(xt_copied, g)
                    if g == 1:
                        project(0)
                    project(g)
            pe.wait_ge(xt_copied, STEPS)
            project(STEPS)

            def scores(i, j, first):
                c = j // 2
                place = ps_scores[c % 2][:, j % 2 * BANK:(j % 2 + 1) * BANK]
                cols = slice(j * BANK, (j + 1) * BANK)
                rows = bass.ds(i * P, P)
                if j % 2 == 0 and not (first and c < 2):
                    pe.wait_ge(masked_ready, PIECES * i + c - 1)
                if first:
                    pe.wait_ge(proj_lo, j + 2)
                nc.tensor.matmul(place, q_hi[:, rows], k_hi[:, cols], start=True, stop=False)
                nc.tensor.matmul(place, q_hi[:, rows], k_lo[:, cols], start=False, stop=False)
                last = nc.tensor.matmul(place, q_lo[:, rows], k_hi[:, cols], start=False, stop=True)
                if j % 2 == 1:
                    last.then_inc(scores_ready, 1)

            def transposes(i, s, g, first):
                pe.wait_ge(exp_done, PIECES * i + g // 2 + 1)
                if not (first and g < 2):
                    pe.wait_ge(plo_ready, STEPS * i + g - 1)
                for b in range(BLOCKS):
                    k = g * BLOCKS + b
                    last = nc.tensor.transpose(ps_t[g % 2][:, b * P:(b + 1) * P], s_sb[s][:, k * P:(k + 1) * P], ident[:, :])
                last.then_inc(pt_ready, 1)

            def values(i, s, g):
                pe.wait_ge(plo_ready, STEPS * i + g + 1)
                for b in range(BLOCKS):
                    k = g * BLOCKS + b
                    blk = slice(b * P, (b + 1) * P)
                    nc.tensor.matmul(ps_out[s][:, 0:2 * D + 1], p_hi[:, g % PSLOTS, blk], v_parts[:, k, 0:2 * D + 1],
                                     start=(k == 0), stop=False)
                    last = nc.tensor.matmul(ps_out[s][:, D:2 * D + 1], p_lo[:, g % PSLOTS, blk], v_parts[:, k, D:2 * D + 1],
                                            start=False, stop=(k == TILES - 1))
                last.then_inc(pv_done, 1)

            def period(i, s, has_scores=True, has_last=True, has_first=True, warm=True):
                for j in range(STEPS):
                    if has_scores:
                        scores(i, j, not warm and s == 0)
                    if not warm:
                        for n in proj_of_step.get(STEPS * i + j, ()):
                            project(n)
                        if STEPS * i + j == len(proj_of_step):
                            pe.wait_ge(proj_lo, len(proj))
                    g = (j - LAG_T) % STEPS
                    if j < LAG_T - STEPS and has_last:
                        transposes(i - 2, s, g, False)
                    if j >= LAG_T - STEPS and has_first:
                        transposes(i - 1, 1 - s, g, not warm)
                    g = (j - LAG_PV) % STEPS
                    if j < LAG_PV - STEPS and has_last:
                        values(i - 2, s, g)
                    if j >= LAG_PV - STEPS and has_first:
                        values(i - 1, 1 - s, g)

            period(0, 0, has_last=False, has_first=False, warm=False)
            period(1, 1, has_last=False, warm=False)
            with pe.Fori(1, TILES // 2) as pair:
                for n in range(2):
                    period(2 * pair + n, n)
            period(TILES, 0, has_scores=False)
            period(TILES + 1, 1, has_scores=False, has_first=False)


_INS = ["x", "adj", "L0_gnn_Wq", "L0_gnn_bq", "L0_gnn_Wk", "L0_gnn_bk", "L0_gnn_Wv", "L0_gnn_bv"]


def kernel(**inputs):
    import numpy as _np
    import concourse.bacc as _bacc
    from concourse.bass_utils import run_bass_kernel_spmd as _run

    nc = _bacc.Bacc("TRN2", target_bir_lowering=False, num_devices=1)
    arrays, args = {}, []
    for name in _INS:
        a = _np.ascontiguousarray(inputs[name])
        arrays[f"in_{name}_dram"] = a
        args.append(nc.dram_tensor(f"in_{name}_dram", a.shape, mybir.dt.from_np(a.dtype), kind="ExternalInput").ap())
    out = nc.dram_tensor("out_0_dram", inputs["x"].shape, F32, kind="ExternalOutput").ap()
    attention_kernel(nc, *args, out)
    r = _run(nc, [arrays], core_ids=[0])
    return r.results[0]["out_0_dram"]
```

```python
from contextlib import ExitStack

import concourse.bass as bass
from concourse import mybir

ALU = mybir.AluOpType
ACT = mybir.ActivationFunctionType
AX_X = mybir.AxisListType.X
F32 = mybir.dt.float32
F16 = mybir.dt.float16
I32 = mybir.dt.int32

P = 128
STEPS = 8
BANK = 512
PIECE = 2 * BANK
MASKED = -9000000000000000.0
EPS = 1e-5
P_SCALE = 2.0 ** 15
LAG_T = STEPS + 3
LAG_LO = STEPS + 4
LAG_PV = STEPS + 5
PSLOTS = 4
POOL_OPS = 11
HAS_ATT, HAS_Y, HAS_MEAN = 2, 5, 6


def attention_kernel(nc, x, adj, wq, bq, wk, bk, wv, bv, out):
    N, D = x.shape
    TILES = N // P
    PIECES = N // PIECE
    BLOCKS = BANK // P
    SCALE = float(D) ** -0.5
    VW = 2 * D + 2
    assert D == P and N == STEPS * BANK and TILES % 2 == 0

    with ExitStack() as ctx:
        def sb(name, shape, dt):
            return ctx.enter_context(nc.sbuf_tensor(name, shape, dt))

        def psum(name, shape):
            return ctx.enter_context(nc.psum_tensor(name, shape, F32))

        def sem(name):
            return ctx.enter_context(nc.semaphore(name))

        ps_scores = [psum(f"ps_scores{n}", [P, PIECE]) for n in range(2)]
        ps_t = [psum(f"ps_t{n}", [P, BANK]) for n in range(2)]
        ps_out = [psum(f"ps_out{n}", [P, BANK]) for n in range(2)]

        x_rows = sb("x_rows", [P, TILES, D], F32)
        x_t = sb("x_t", [P, N], F32)
        w_rows = sb("w_rows", [P, 3, D], F32)
        w_t = sb("w_t", [P, 3, D], F32)
        b_cols = sb("b_cols", [P, 2], F32)
        bv_rows = sb("bv_rows", [P, D], F32)
        ident = sb("ident", [P, P], F32)
        q_hi = sb("q_hi", [P, N], F16)
        q_lo = sb("q_lo", [P, N], F16)
        k_hi = sb("k_hi", [P, N], F16)
        k_lo = sb("k_lo", [P, N], F16)
        v_parts = sb("v_parts", [P, TILES, VW], F16)
        v_sb = sb("v_sb", [P, 2, BLOCKS, D], F32)
        adj_sb = [sb(f"adj{n}", [P, N], I32) for n in range(2)]
        mask_sb = [a[:, :].bitcast(F32) for a in adj_sb]
        s_sb = [sb(f"scores{n}", [P, N], F32) for n in range(2)]
        max_parts = sb("max_parts", [P, 2, PIECES], F32)
        neg_max = sb("neg_max", [P, 2], F32)
        p_hi = sb("p_hi", [P, PSLOTS, BANK], F16)
        p_lo = sb("p_lo", [P, PSLOTS, BANK], F16)
        recip = sb("recip", [P, 2], F32)
        att2 = sb("att2", [P, 2, 2 * D], F32)
        att_sum = sb("att_sum", [P, 2, D], F32)
        att = sb("att", [P, 2, D], F32)
        neg = sb("neg", [P, 2, D], F32)
        pos = sb("pos", [P, 2, D], F32)
        exp_neg = sb("exp_neg", [P, 2, D], F32)
        res = sb("res", [P, 2, D], F32)
        y = sb("y", [P, 2, D], F32)
        act_junk = sb("act_junk", [P, D], F32)
        y_sum = sb("y_sum", [P, 2], F32)
        neg_mean = sb("neg_mean", [P, 2], F32)
        sq_sum = sb("sq_sum", [P, 2], F32)
        var = sb("var", [P, 2], F32)
        rstd = sb("rstd", [P, 2], F32)
        stat_consts = sb("stat_consts", [P, 5], F32)
        expm1 = sb("expm1", [P, 2, D], F32)
        var_eps = sb("var_eps", [P, 2], F32)
        centred = sb("centred", [P, 2, D], F32)
        y_out = sb("y_out", [P, 2, D], F32)

        w_in = sem("w_in")
        b_in = sem("b_in")
        bv_in = sem("bv_in")
        x_in = [sem(f"x_in{n}") for n in range(4)]
        consts_set = sem("consts_set")
        ident_set = sem("ident_set")
        wt_ready = sem("wt_ready")
        wt_copied = sem("wt_copied")
        xt_ready = sem("xt_ready")
        xt_copied = sem("xt_copied")
        proj_ready = sem("proj_ready")
        proj_hi = sem("proj_hi")
        proj_lo = sem("proj_lo")
        v_ready = sem("v_ready")
        v_copied = sem("v_copied")
        v_lo = sem("v_lo")
        adj_in = [[sem(f"adj_in{n}_{c}") for c in range(PIECES)] for n in range(2)]
        mask_ready = sem("mask_ready")
        scores_ready = sem("scores_ready")
        masked_ready = sem("masked_ready")
        max_ready = sem("max_ready")
        exp_done = sem("exp_done")
        pt_ready = sem("pt_ready")
        phi_ready = sem("phi_ready")
        plo_ready = sem("plo_ready")
        pv_done = sem("pv_done")
        recip_ready = sem("recip_ready")
        att_ready = sem("att_ready")
        relu_ready = sem("relu_ready")
        expneg_ready = sem("expneg_ready")
        ysum_ready = sem("ysum_ready")
        sqsum_ready = sem("sqsum_ready")
        pool_done = sem("pool_done")
        stored = [sem(f"stored{n}") for n in range(2)]

        x_tiled = x.rearrange("(t p) d -> p t d", p=P)
        adj_tiled = adj.rearrange("(t p) m -> t p m", p=P)
        out_tiled = out.rearrange("(t p) d -> t p d", p=P)
        XQ = TILES // 4

        def ps_xt(g):
            return ps_scores[g // 2 % 2][:, g % 2 * BANK:(g % 2 + 1) * BANK]

        ps_proj = ps_t + ps_out
        proj = [("q", 0, 3)] + [("k", g, g % 4) for g in range(STEPS)]
        AHEAD = len(proj)
        proj += [("q", g, g % 2) for g in range(1, STEPS)]

        def q_at(t):
            return [AHEAD + t - 4] if 0 <= t - 4 < STEPS - 1 else []

        def v_at(t):
            return [t - 1] if 0 <= t - 1 < STEPS else []

        def user_before(n):
            return max([m + 1 for m in range(n) if proj[m][2] == proj[n][2]], default=0)

        def last_user(bank):
            return 1 + max(n for n, p in enumerate(proj) if p[2] == bank)

        def ps_v(g):
            return ps_out[g % 2]

        block = ctx.enter_context(nc.Block())

        @block.sync
        def _(sp):
            for n in range(4):
                if n == 1:
                    sp.dma_start(w_rows[:, 1, :], wk).then_inc(w_in, 16)
                    sp.dma_start(w_rows[:, 0, :], wq).then_inc(w_in, 16)
                    sp.dma_start(w_rows[:, 2, :], wv).then_inc(w_in, 16)
                sp.dma_start(x_rows[:, n * XQ:(n + 1) * XQ, :], x_tiled[:, n * XQ:(n + 1) * XQ, :]).then_inc(x_in[n], 16)

            def load(i, slot, first):
                for c in range(PIECES):
                    if not first:
                        sp.wait_ge(masked_ready, PIECES * (i - 2) + c + 1)
                    cols = slice(c * PIECE, (c + 1) * PIECE)
                    sp.dma_start(adj_sb[slot][:, cols], adj_tiled[i, :, cols]).then_inc(adj_in[slot][c], 16)

            def store(i, slot):
                sp.wait_ge(pool_done, POOL_OPS * (i + 1))
                sp.dma_start(out_tiled[i], y_out[:, slot, :]).then_inc(stored[slot], 16)

            load(0, 0, True)
            load(1, 1, True)
            load(2, 0, False)
            load(3, 1, False)
            with sp.Fori(1, TILES // 2 - 1) as pair:
                for n in range(2):
                    load(2 * pair + n + 2, n, False)
                    store(2 * pair + n - 2, n)
            for i in range(TILES - 4, TILES):
                store(i, i % 2)
            for n in range(2):
                sp.wait_ge(stored[n], 16 * (TILES // 2))

        @block.gpsimd
        def _(pool):
            nc.gpsimd.memset(ident[:, :], 0.0).then_inc(consts_set, 1)
            for n, value in enumerate((-1.0 / D, 1.0 / D, EPS, -0.5, -1.0)):
                nc.gpsimd.memset(stat_consts[:, n:n + 1], value).then_inc(consts_set, 1)
            nc.gpsimd.memset(v_parts[:, :, 2 * D:VW], 1.0).then_inc(consts_set, 1)
            pool.wait_ge(consts_set, 7)
            nc.gpsimd.affine_select(out=ident[:, :], in_=ident[:, :], compare_op=ALU.not_equal, fill=1.0,
                                    base=0, pattern=[[-1, P]], channel_multiplier=1).then_inc(ident_set, 1)

            for g in range(STEPS):
                rows = slice(g * BLOCKS, (g + 1) * BLOCKS)
                pool.wait_ge(v_copied, 2 * g + 2)
                nc.gpsimd.tensor_tensor(v_parts[:, rows, 0:D], v_sb[:, g % 2], v_parts[:, rows, D:2 * D],
                                        ALU.subtract).then_inc(v_lo, 1)

            def finish(i, s):
                one = slice(s, s + 1)
                base = POOL_OPS * i
                pool.wait_ge(att_ready, i + 1)
                nc.gpsimd.tensor_tensor(att_sum[:, s, :], att2[:, s, 0:D], att2[:, s, D:2 * D], ALU.add).then_inc(pool_done, 1)
                pool.wait_ge(pool_done, base + 1)
                nc.gpsimd.tensor_tensor(att[:, s, :], att_sum[:, s, :], bv_rows[:, :], ALU.add).then_inc(pool_done, 1)
                pool.wait_ge(relu_ready, 2 * i + 1)
                nc.gpsimd.tensor_tensor(res[:, s, :], pos[:, s, :], x_rows[:, bass.ds(i, 1), :], ALU.add).then_inc(pool_done, 1)
                pool.wait_ge(expneg_ready, i + 1)
                nc.gpsimd.tensor_tensor(expm1[:, s, :], exp_neg[:, s, :], stat_consts[:, 4:5].to_broadcast([P, D]),
                                        ALU.add).then_inc(pool_done, 1)
                pool.wait_ge(pool_done, base + 4)
                nc.gpsimd.tensor_tensor(y[:, s, :], res[:, s, :], expm1[:, s, :], ALU.add).then_inc(pool_done, 1)
                pool.wait_ge(ysum_ready, i + 1)
                nc.gpsimd.tensor_tensor(neg_mean[:, one], y_sum[:, one], stat_consts[:, 0:1], ALU.mult).then_inc(pool_done, 1)
                pool.wait_ge(pool_done, base + 6)
                nc.gpsimd.tensor_tensor(centred[:, s, :], y[:, s, :], neg_mean[:, one].to_broadcast([P, D]),
                                        ALU.add).then_inc(pool_done, 1)
                pool.wait_ge(sqsum_ready, i + 1)
                nc.gpsimd.tensor_tensor(var[:, one], sq_sum[:, one], stat_consts[:, 1:2], ALU.mult).then_inc(pool_done, 1)
                pool.wait_ge(pool_done, base + 8)
                nc.gpsimd.tensor_tensor(var_eps[:, one], var[:, one], stat_consts[:, 2:3], ALU.add).then_inc(pool_done, 1)
                pool.wait_ge(pool_done, base + 9)
                nc.gpsimd.tensor_tensor(rstd[:, one], var_eps[:, one], stat_consts[:, 3:4], ALU.pow).then_inc(pool_done, 1)
                pool.wait_ge(pool_done, base + 10)
                nc.gpsimd.tensor_tensor(y_out[:, s, :], centred[:, s, :], rstd[:, one].to_broadcast([P, D]),
                                        ALU.mult).then_inc(pool_done, 1)

            def finish_tile(i, s, first):
                if not first:
                    pool.wait_ge(stored[s], 8 * (i - s))
                finish(i, s)

            pool.wait_ge(bv_in, 16)
            finish_tile(0, 0, True)
            finish_tile(1, 1, True)
            with pool.Fori(1, TILES // 2) as pair:
                for n in range(2):
                    finish_tile(2 * pair + n, n, False)

        @block.scalar
        def _(act):
            act.dma_start(b_cols[:, 0:1], bq.rearrange("(p a) -> p a", a=1)).then_inc(b_in, 16)
            act.dma_start(b_cols[:, 1:2], bk.rearrange("(p a) -> p a", a=1)).then_inc(b_in, 16)
            act.dma_start(bv_rows[:, :], bv.rearrange("(a d) -> a d", a=1).to_broadcast([P, D])).then_inc(bv_in, 16)

            def copy_x(g):
                act.wait_ge(xt_ready, g + 1)
                nc.scalar.activation(x_t[:, g * BANK:(g + 1) * BANK], ps_xt(g), ACT.Copy).then_inc(xt_copied, 1)

            def high_of_projection(n):
                which, g, bank = proj[n]
                cols = slice(g * BANK, (g + 1) * BANK)
                act.wait_ge(proj_ready, n + 1)
                if which == "k":
                    ins = nc.scalar.activation(k_hi[:, cols], ps_proj[bank][:, :], ACT.Identity, bias=b_cols[:, 1:2])
                else:
                    ins = nc.scalar.activation(q_hi[:, cols], ps_proj[bank][:, :], ACT.Identity, bias=b_cols[:, 0:1])
                ins.then_inc(proj_hi, 1)

            def copy_v(g):
                act.wait_ge(v_ready, g + 1)
                if g >= 2:
                    act.wait_ge(v_lo, g - 1)
                v = ps_v(g)[:, :].rearrange("p (b d) -> p b d", d=D)
                nc.scalar.activation(v_sb[:, g % 2], v, ACT.Copy).then_inc(v_copied, 1)
                nc.scalar.activation(v_parts[:, g * BLOCKS:(g + 1) * BLOCKS, D:2 * D], v, ACT.Copy).then_inc(v_copied, 1)

            copy_x(0)
            copy_x(1)
            act.wait_ge(wt_ready, 1)
            nc.scalar.activation(w_t[:, :, :], ps_t[0][:, 0:3 * D].rearrange("p (n d) -> p n d", d=D), ACT.Copy).then_inc(wt_copied, 1)
            act.wait_ge(b_in, 16 * 2)
            for g in range(2, STEPS + 2):
                if g < STEPS:
                    copy_x(g)
                if g == 2:
                    high_of_projection(0)
                high_of_projection(g - 1)

            def exp_piece(i, s, c):
                if c == 0:
                    act.wait_ge(max_ready, i + 1)
                cols = slice(c * PIECE, (c + 1) * PIECE)
                nc.scalar.activation(s_sb[s][:, cols], s_sb[s][:, cols], ACT.Exp,
                                     bias=neg_max[:, s:s + 1]).then_inc(exp_done, 1)

            def high_part(i, g, first):
                act.wait_ge(pt_ready, STEPS * i + g + 1)
                if not first:
                    act.wait_ge(pv_done, STEPS * i + g + 1 - PSLOTS)
                nc.scalar.activation(p_hi[:, g % PSLOTS, :], ps_t[g % 2][:, :], ACT.Copy, scale=P_SCALE).then_inc(phi_ready, 1)

            def attention(i, s):
                act.wait_ge(recip_ready, i + 1)
                nc.scalar.activation(att2[:, s, :], ps_out[s][:, 0:2 * D], ACT.Copy, scale=recip[:, s:s + 1]).then_inc(att_ready, 1)

            def elu_exp(i, s):
                act.wait_ge(pool_done, POOL_OPS * i + HAS_ATT)
                nc.scalar.activation(pos[:, s, :], att[:, s, :], ACT.Relu).then_inc(relu_ready, 1)
                nc.scalar.activation(neg[:, s, :], att[:, s, :], ACT.Relu, scale=-1.0).then_inc(relu_ready, 1)
                act.wait_ge(relu_ready, 2 * i + 2)
                nc.scalar.activation(exp_neg[:, s, :], neg[:, s, :], ACT.Exp, scale=-1.0).then_inc(expneg_ready, 1)

            def row_sum(i, s):
                act.wait_ge(pool_done, POOL_OPS * i + HAS_Y)
                nc.scalar.activation(act_junk[:, :], y[:, s, :], ACT.Copy, accum_out=y_sum[:, s:s + 1]).then_inc(ysum_ready, 1)

            def square_sum(i, s):
                act.wait_ge(pool_done, POOL_OPS * i + HAS_MEAN)
                nc.scalar.activation(act_junk[:, :], y[:, s, :], ACT.Square, bias=neg_mean[:, s:s + 1],
                                     accum_out=sq_sum[:, s:s + 1]).then_inc(sqsum_ready, 1)

            def period(i, s, has_exp=True, has_last=True, has_first=True, warm=True, ends=((0, 5),)):
                for j in range(STEPS):
                    if not warm:
                        for g in v_at(STEPS * i + j):
                            copy_v(g)
                        for n in q_at(STEPS * i + j):
                            high_of_projection(n)
                    g = (j - LAG_T) % STEPS
                    if j < LAG_T - STEPS and has_last:
                        high_part(i - 2, g, False)
                    if j >= LAG_T - STEPS and has_first:
                        high_part(i - 1, g, not warm and g < PSLOTS)
                    for back, step in ends:
                        if has_last:
                            ending = (i - 2 - back, s ^ (back % 2))
                            if j == step:
                                attention(*ending)
                            if j == step + 1:
                                elu_exp(*ending)
                            if j == step + 2:
                                row_sum(*ending)
                    if j % 2 == 1 and has_exp:
                        exp_piece(i - 1, 1 - s, j // 2)
                    for back, step in ends:
                        if has_last and j == step + 2:
                            square_sum(i - 2 - back, s ^ (back % 2))

            period(0, 0, has_exp=False, has_last=False, has_first=False, warm=False)
            period(1, 1, has_last=False, warm=False)
            with act.Fori(1, TILES // 2) as pair:
                for n in range(2):
                    period(2 * pair + n, n)
            period(TILES, 0, ends=())
            period(TILES + 1, 1, has_exp=False, has_first=False, ends=((1, 0), (0, 5)))

        @block.vector
        def _(dve):
            def low_of_projection(n):
                which, g, bank = proj[n]
                cols = slice(g * BANK, (g + 1) * BANK)
                dve.wait_ge(proj_hi, n + 1)
                if which == "k":
                    ins = nc.vector.scalar_tensor_tensor(out=k_lo[:, cols], in0=ps_proj[bank][:, :], scalar=b_cols[:, 1:2],
                                                         in1=k_hi[:, cols], op0=ALU.add, op1=ALU.subtract)
                else:
                    ins = nc.vector.scalar_tensor_tensor(out=q_lo[:, cols], in0=ps_proj[bank][:, :], scalar=b_cols[:, 0:1],
                                                         in1=q_hi[:, cols], op0=ALU.add, op1=ALU.subtract)
                ins.then_inc(proj_lo, 1)

            def mask_piece(i, s, c):
                cols = slice(c * PIECE, (c + 1) * PIECE)
                dve.wait_ge(adj_in[s][c], 8 * (i - s) + 16)
                nc.vector.tensor_scalar(mask_sb[s][:, cols], adj_sb[s][:, cols], 0.0, MASKED / SCALE,
                                        ALU.is_le, ALU.mult).then_inc(mask_ready, 1)

            def masked_piece(i, s, c, first, makes_mask):
                cols = slice(c * PIECE, (c + 1) * PIECE)
                if not first:
                    dve.wait_ge(pt_ready, STEPS * (i - 2) + 2 * c + 2)
                dve.wait_ge(mask_ready, PIECES * i + c + 1)
                dve.wait_ge(scores_ready, PIECES * i + c + 1)
                if makes_mask:
                    mask_piece(i + 1, 1 - s, c)
                nc.vector.tensor_tensor_reduce(out=s_sb[s][:, cols], in0=ps_scores[c % 2][:, :], in1=mask_sb[s][:, cols],
                                               scale=SCALE, scalar=-3.0e38, op0=ALU.add, op1=ALU.max,
                                               accum_out=max_parts[:, s, c:c + 1]).then_inc(masked_ready, 1)

            def row_max(i, s):
                dve.wait_ge(masked_ready, PIECES * (i + 1))
                nc.vector.tensor_reduce(neg_max[:, s:s + 1], max_parts[:, s, :], AX_X, ALU.max,
                                        negate=True).then_inc(max_ready, 1)

            def low_part(i, g):
                dve.wait_ge(phi_ready, STEPS * i + g + 1)
                nc.vector.scalar_tensor_tensor(out=p_lo[:, g % PSLOTS, :], in0=ps_t[g % 2][:, :], scalar=P_SCALE,
                                               in1=p_hi[:, g % PSLOTS, :], op0=ALU.mult, op1=ALU.subtract).then_inc(plo_ready, 1)

            def reciprocal(i, s):
                dve.wait_ge(pv_done, STEPS * (i + 1))
                nc.vector.reciprocal(recip[:, s:s + 1], ps_out[s][:, 2 * D:2 * D + 1]).then_inc(recip_ready, 1)

            def period(i, s, has_scores=True, has_last=True, has_first=True, warm=True, makes_mask=True):
                for j in range(STEPS):
                    if not warm:
                        for n in q_at(STEPS * i + j):
                            low_of_projection(n)
                    g = (j - LAG_LO) % STEPS
                    if j < LAG_LO - STEPS and has_last:
                        low_part(i - 2, g)
                    if j >= LAG_LO - STEPS and has_first:
                        low_part(i - 1, g)
                    if j == 5 and has_last:
                        reciprocal(i - 2, s)
                    if has_scores:
                        if j % 2 == 1:
                            masked_piece(i, s, j // 2, not warm, makes_mask)
                        if j == STEPS - 1:
                            row_max(i, s)

            for n in range(AHEAD):
                low_of_projection(n)
                if n >= AHEAD - PIECES:
                    mask_piece(0, 0, n - AHEAD + PIECES)
            period(0, 0, has_last=False, has_first=False, warm=False)
            period(1, 1, has_last=False, warm=False)
            with dve.Fori(1, TILES // 2 - 1) as pair:
                for n in range(2):
                    period(2 * pair + n, n)
            period(TILES - 2, 0)
            period(TILES - 1, 1, makes_mask=False)
            period(TILES, 0, has_scores=False)
            period(TILES + 1, 1, has_scores=False, has_first=False)

        @block.tensor
        def _(pe):
            def project(n):
                which, g, bank = proj[n]
                if user_before(n):
                    pe.wait_ge(proj_lo, user_before(n))
                nc.tensor.matmul(ps_proj[bank][:, :], w_t[:, "qk".index(which), :], x_t[:, g * BANK:(g + 1) * BANK],
                                 start=True, stop=True).then_inc(proj_ready, 1)

            def project_v(g):
                if g < 2:
                    pe.wait_ge(proj_lo, last_user(2 + g))
                else:
                    pe.wait_ge(v_copied, 2 * g - 2)
                for b in range(BLOCKS):
                    t = g * BLOCKS + b
                    last = nc.tensor.matmul(ps_v(g)[:, b * D:(b + 1) * D], x_t[:, t * P:(t + 1) * P], w_t[:, 2, :],
                                            start=True, stop=True)
                last.then_inc(v_ready, 1)

            def transpose_x(g):
                if g % 2 == 0:
                    pe.wait_ge(x_in[g // 2], 16)
                if g >= 4:
                    pe.wait_ge(xt_copied, g - 3)
                for b in range(BLOCKS):
                    last = nc.tensor.transpose(ps_xt(g)[:, b * P:(b + 1) * P], x_rows[:, g * BLOCKS + b, :], ident[:, :])
                last.then_inc(xt_ready, 1)

            pe.wait_ge(ident_set, 1)
            transpose_x(0)
            transpose_x(1)
            pe.wait_ge(w_in, 16 * 3)
            for n in range(3):
                last = nc.tensor.transpose(ps_t[0][:, n * D:(n + 1) * D], w_rows[:, n, :], ident[:, :])
            last.then_inc(wt_ready, 1)
            for g in range(2, STEPS + 2):
                if g < STEPS:
                    transpose_x(g)
                if g == 2:
                    pe.wait_ge(wt_copied, 1)
                    pe.wait_ge(xt_copied, 1)
                    project(0)
                pe.wait_ge(xt_copied, g - 1)
                project(g - 1)

            def scores(i, j, first):
                c = j // 2
                place = ps_scores[c % 2][:, j % 2 * BANK:(j % 2 + 1) * BANK]
                cols = slice(j * BANK, (j + 1) * BANK)
                rows = bass.ds(i * P, P)
                if j % 2 == 0 and not (first and c < 2):
                    pe.wait_ge(masked_ready, PIECES * i + c - 1)
                if first:
                    pe.wait_ge(proj_lo, j + 2)
                nc.tensor.matmul(place, q_hi[:, rows], k_hi[:, cols], start=True, stop=False)
                nc.tensor.matmul(place, q_hi[:, rows], k_lo[:, cols], start=False, stop=False)
                last = nc.tensor.matmul(place, q_lo[:, rows], k_hi[:, cols], start=False, stop=True)
                if j % 2 == 1:
                    last.then_inc(scores_ready, 1)

            def transposes(i, s, g, first):
                pe.wait_ge(exp_done, PIECES * i + g // 2 + 1)
                if first and g < 2:
                    pe.wait_ge(proj_lo, last_user(g))
                if not (first and g < 2):
                    pe.wait_ge(plo_ready, STEPS * i + g - 1)
                for b in range(BLOCKS):
                    k = g * BLOCKS + b
                    last = nc.tensor.transpose(ps_t[g % 2][:, b * P:(b + 1) * P], s_sb[s][:, k * P:(k + 1) * P], ident[:, :])
                last.then_inc(pt_ready, 1)

            def values(i, s, g, first):
                pe.wait_ge(plo_ready, STEPS * i + g + 1)
                if first:
                    pe.wait_ge(v_copied, 2 * STEPS)
                    pe.wait_ge(v_lo, g + 1)
                for b in range(BLOCKS):
                    k = g * BLOCKS + b
                    blk = slice(b * P, (b + 1) * P)
                    nc.tensor.matmul(ps_out[s][:, 0:2 * D + 1], p_hi[:, g % PSLOTS, blk], v_parts[:, k, 0:2 * D + 1],
                                     start=(k == 0), stop=False)
                    last = nc.tensor.matmul(ps_out[s][:, D:2 * D + 1], p_lo[:, g % PSLOTS, blk], v_parts[:, k, D:2 * D + 1],
                                            start=False, stop=(k == TILES - 1))
                last.then_inc(pv_done, 1)

            def period(i, s, has_scores=True, has_last=True, has_first=True, warm=True):
                for j in range(STEPS):
                    if has_scores:
                        scores(i, j, not warm and s == 0)
                    if not warm:
                        for g in v_at(STEPS * i + j):
                            project_v(g)
                        for n in q_at(STEPS * i + j):
                            project(n)
                    g = (j - LAG_T) % STEPS
                    if j < LAG_T - STEPS and has_last:
                        transposes(i - 2, s, g, False)
                    if j >= LAG_T - STEPS and has_first:
                        transposes(i - 1, 1 - s, g, not warm)
                    g = (j - LAG_PV) % STEPS
                    if j < LAG_PV - STEPS and has_last:
                        values(i - 2, s, g, False)
                    if j >= LAG_PV - STEPS and has_first:
                        values(i - 1, 1 - s, g, not warm)

            period(0, 0, has_last=False, has_first=False, warm=False)
            period(1, 1, has_last=False, warm=False)
            pe.wait_ge(proj_lo, len(proj))
            pe.wait_ge(v_lo, STEPS)
            with pe.Fori(1, TILES // 2) as pair:
                for n in range(2):
                    period(2 * pair + n, n)
            period(TILES, 0, has_scores=False)
            period(TILES + 1, 1, has_scores=False, has_first=False)


_INS = ["x", "adj", "L0_gnn_Wq", "L0_gnn_bq", "L0_gnn_Wk", "L0_gnn_bk", "L0_gnn_Wv", "L0_gnn_bv"]


def kernel(**inputs):
    import numpy as _np
    import concourse.bacc as _bacc
    from concourse.bass_utils import run_bass_kernel_spmd as _run

    nc = _bacc.Bacc("TRN2", target_bir_lowering=False, num_devices=1)
    arrays, args = {}, []
    for name in _INS:
        a = _np.ascontiguousarray(inputs[name])
        arrays[f"in_{name}_dram"] = a
        args.append(nc.dram_tensor(f"in_{name}_dram", a.shape, mybir.dt.from_np(a.dtype), kind="ExternalInput").ap())
    out = nc.dram_tensor("out_0_dram", inputs["x"].shape, F32, kind="ExternalOutput").ap()
    attention_kernel(nc, *args, out)
    r = _run(nc, [arrays], core_ids=[0])
    return r.results[0]["out_0_dram"]
```
